# Optimizing a Trainium2 kernel written in Bass

```python
import numpy as np
import jax
import jax.numpy as jnp

def _softmax(x, axis=-1):
    return jax.nn.softmax(x, axis=axis)

def _gelu(x):
    return jax.nn.gelu(x, approximate=True)

def _silu(x):
    return jax.nn.silu(x)

def _sigmoid(x):
    return jax.nn.sigmoid(x)

def _layernorm(x, axis=-1, eps=1e-05):
    m = jnp.mean(x, axis=axis, keepdims=True)
    v = jnp.var(x, axis=axis, keepdims=True)
    return (x - m) / jnp.sqrt(v + eps)

def _scatter_add(tgt, idx, src, axis=0):
    return tgt.at[idx].add(src)

def _segment_sum(src, seg, n):
    return jax.ops.segment_sum(src, seg, n)
kernel_name = 'mk_prb_d1_jaxref_r4_e9b5a7'

def setup_inputs(seed: int=0):
    np.random.seed(seed)
    _w = jnp.asarray

    def _L0_attn_setup():
        import jax, jax.numpy as jnp
        import numpy as np
        D_MODEL = 256
        N_HEAD = 16
        SEQ = 512
        BATCH = 2
        key = jax.random.key(seed)
        x = jax.random.normal(key, (BATCH, SEQ, D_MODEL), dtype=jnp.float32)
        return {'x': x}
    _L0_attn_in = _L0_attn_setup()

    def _L0_ffn_setup():
        import jax, jax.numpy as jnp
        import numpy as np
        LORA_DIM = 16
        LORA_TOKEN_INDEX = 1
        B, S, D, H = (4, 512, 256, 1024)
        key = jax.random.key(seed)
        ks = jax.random.split(key, 6)
        x = jax.random.normal(ks[0], (B, S, D), dtype=jnp.float32)
        W1 = jax.random.normal(ks[1], (H, D), dtype=jnp.float32) * 0.02
        b1 = jnp.zeros((H,), dtype=jnp.float32)
        W2 = jax.random.normal(ks[2], (D, H), dtype=jnp.float32) * 0.02
        b2 = jnp.zeros((D,), dtype=jnp.float32)
        scale = jnp.asarray(0.001, dtype=jnp.float32)
        return {'x': x, 'W1': W1, 'b1': b1, 'W2': W2, 'b2': b2, 'scale': scale}
    _L0_ffn_in = _L0_ffn_setup()
    _d = {'L0_attn_x': _L0_attn_in['x'], 'L0_ffn_W1': _L0_ffn_in['W1'], 'L0_ffn_b1': _L0_ffn_in['b1'], 'L0_ffn_W2': _L0_ffn_in['W2'], 'L0_ffn_b2': _L0_ffn_in['b2'], 'L0_ffn_scale': _L0_ffn_in['scale']}
    _x0 = _d['L0_attn_x']
    _d['L0_attn_x'] = jax.random.normal(jax.random.fold_in(jax.random.key(seed), 1), (8, 1024, 256), dtype=_x0.dtype)
    del _x0
    return _d

def reference(L0_attn_x, L0_ffn_W1, L0_ffn_b1, L0_ffn_W2, L0_ffn_b2, L0_ffn_scale):

    def _L0_attn_ref(x):
        import jax, jax.numpy as jnp
        import numpy as np
        D_MODEL = 256
        N_HEAD = 16
        SEQ = 512
        BATCH = 2
        B, S, D = x.shape
        H = N_HEAD
        hd = D // H
        qkv = x.reshape(B, S, H, hd).transpose(0, 2, 1, 3)
        q = k = v = qkv
        w = jnp.einsum('bhqd,bhkd->bhqk', q, k) / jnp.sqrt(jnp.asarray(hd, x.dtype))
        causal = jnp.tril(jnp.ones((S, S), dtype=bool))
        mask_value = jnp.finfo(w.dtype).min
        w = jnp.where(causal[None, None, :, :], w, mask_value)
        w = jax.nn.softmax(w, axis=-1)
        out = jnp.einsum('bhqk,bhkd->bhqd', w, v)
        return out.transpose(0, 2, 1, 3).reshape(B, S, D)

    def _L0_ffn_ref(x, W1, b1, W2, b2, scale):
        import jax, jax.numpy as jnp
        import numpy as np
        LORA_DIM = 16
        LORA_TOKEN_INDEX = 1
        B, S, D, H = (4, 512, 256, 1024)
        Bx, Sx, Dx = x.shape
        Hx = W1.shape[0]
        lt = jax.lax.dynamic_slice_in_dim(x, LORA_TOKEN_INDEX, LORA_DIM, axis=1)
        even = lt[:, ::2, :]
        odd = lt[:, 1::2, :]
        m1 = (even[:, :4, :, None] * odd[:, :4, None, :]).reshape(Bx, Hx, Dx)
        m2 = (even[:, 4:, :, None] * odd[:, 4:, None, :]).reshape(Bx, Dx, Hx)
        h = jnp.einsum('bsd,hd->bsh', x, W1) + scale * jnp.einsum('bsd,bhd->bsh', x, m1) + b1
        h = jax.nn.gelu(h, approximate=False)
        out = jnp.einsum('bsh,oh->bso', h, W2) + scale * jnp.einsum('bsh,boh->bso', h, m2) + b2
        return out
    x = L0_attn_x
    xn = _layernorm(x, axis=-1)
    x = x + _L0_attn_ref(xn) + _L0_ffn_ref(xn, L0_ffn_W1, L0_ffn_b1, L0_ffn_W2, L0_ffn_b2, L0_ffn_scale)
    return x

_drawn_inputs = setup_inputs


def setup_inputs(seed=0):
    import zlib

    import numpy as np

    out = dict(_drawn_inputs(seed))
    spreads = {'L0_ffn_b1': (0.0, 0.313), 'L0_ffn_b2': (0.0, 0.1)}
    factors = {}
    for name, (base, spread) in spreads.items():
        noise = np.random.default_rng([zlib.crc32(name.encode()), seed]).standard_normal(out[name].shape)
        drawn = base * np.exp(spread * noise) if base else spread * noise
        out[name] = jnp.asarray(drawn.astype(out[name].dtype))
    for name, factor in factors.items():
        out[name] = (out[name] * factor).astype(out[name].dtype)
    return out
```

```python
from contextlib import ExitStack

import concourse.bass as bass
from concourse import mybir

FP32 = mybir.dt.float32
FP32R = mybir.dt.float32r
FP16 = mybir.dt.float16
I32 = mybir.dt.int32
ALU = mybir.AluOpType
ACT = mybir.ActivationFunctionType

B, S, D, HID = 8, 1024, 256, 1024
P = 128
HEADS, HD = 16, 16
NT = S // P
DT = D // P
MT = HID // P
BANK = 512
GH = 4
GROUPS = HEADS // GH
VW = 32
QSCALE = 1024.0
EXP_SCALE = HD ** -0.5 / QSCALE ** 2
EPS = 1e-5
CHUNK = 512
NLORA = 4

SLOTS = [
    [(0, 0, 512)],
    [(1, 128, 384), (3, 384, 128)],
    [(0, 512, 512)],
    [(2, 256, 256), (6, 768, 256)],
    [(1, 512, 512)],
    [(4, 512, 512)],
    [(2, 512, 512)],
    [(5, 640, 384), (7, 896, 128)],
    [(3, 512, 512)],
]
NS = len(SLOTS)
HALF0_DONE = 4
SLOTS_SEQ = NS * GROUPS
LEAD = 2
RING = 3
assert all(sum(n for _, _, n in segs) == BANK for segs in SLOTS)
assert sum(n for segs in SLOTS for _, _, n in segs) == sum(S - P * kb for kb in range(NT))


def columns(slot):
    at = 0
    for kb, q0, n in SLOTS[slot]:
        yield kb, q0, n, at, q0 == kb * P
        at += n


DIAG = [any(c[4] for c in columns(i)) for i in range(NS)]
DIAG_BEFORE = [sum(DIAG[:i]) for i in range(NS + 1)]
DIAG_GROUP = DIAG_BEFORE[NS]


def masks_until(slot):
    return slot // NS * DIAG_GROUP + DIAG_BEFORE[slot % NS]


TILES_0, TILES = 2 * LEAD, 2 * SLOTS_SEQ
MASKS_0, MASKS = masks_until(LEAD), DIAG_GROUP * GROUPS
FFN_CHUNKS = S // CHUNK
XT_USES = 4
TB = CHUNK // P
USES_0 = XT_USES
USES = FFN_CHUNKS * (MT + TB) + 2 * GROUPS + XT_USES
GELUS = FFN_CHUNKS * MT
STACK_DMAS = 3 * GH
PAIR_DMAS = 2 * DT
CONST_DMAS = 3
CHAIN = 52
CHAIN_0 = 16


def attention_ffn(nc, x, w1t, w2t, b1, b2, scale, out):
    ctx = ExitStack()
    with ctx:
        def sb(name, shape, dt=FP32):
            return ctx.enter_context(nc.sbuf_tensor(name, shape, dt))

        def pb(name, shape):
            return ctx.enter_context(nc.psum_tensor(name, shape, FP32))

        def sem(name):
            return ctx.enter_context(nc.semaphore(name))

        pair_dram = nc.dram_tensor("pair_dram", [B, HEADS, 2, HD, S], FP16, kind="Internal").ap()
        even_dram = nc.dram_tensor("even_dram", [B, 2 * NLORA, D], FP32, kind="Internal").ap()

        q_stack = sb("q_stack", [P, 2, 2, S], FP16)
        k_stack = sb("k_stack", [P, 2, GH, S], FP16)
        probs = sb("probs", [P, RING, GH, BANK])
        v_ones = sb("v_ones", [P, NT, HEADS, VW])
        xn = sb("xn", [P, NT, D])
        xt_w2 = sb("xt_w2", [P, DT * S])
        xt = xt_w2[:, :].rearrange("p (t s) -> p t s", t=DT)
        w2 = xt_w2[:, :].rearrange("p (t o) -> p t o", t=MT)
        w1 = sb("w1", [P, DT, HID])
        xt_hi = sb("xt_hi", [P, DT, S], FP32R)
        xt_lo = sb("xt_lo", [P, DT, S], FP32R)
        xt_pair = sb("xt_pair", [P, 2, DT, S], FP16)
        w1_hi = sb("w1_hi", [P, DT, HID], FP32R)
        w1_lo = sb("w1_lo", [P, DT, HID], FP32R)
        w2_hi = sb("w2_hi", [P, MT, D], FP32R)
        w2_lo = sb("w2_lo", [P, MT, D], FP32R)
        gelu = sb("gelu", [P, 2, CHUNK])
        g_hi = sb("g_hi", [P, MT, CHUNK], FP32R)
        g_lo = sb("g_lo", [P, MT, CHUNK], FP32R)
        even = sb("even", [P, 2 * NLORA, D])
        odd = sb("odd", [P, DT, 2 * NLORA])
        acc = sb("acc", [P, NT, D])
        o_sb = sb("o_sb", [P, 2, BANK])
        rden = sb("rden", [P, TB, GH, 1])
        o_norm = sb("o_norm", [P, TB, GH * HD])
        stats = sb("stats", [P, NT, 6])
        mean_var = sb("mean_var", [P, NT, 2])
        var_eps = sb("var_eps", [P, NT, 1])
        rstd = sb("rstd", [P, NT, 1])
        newton = sb("newton", [P, NT, 1])
        ident = sb("ident", [P, P])
        b1_sb = sb("b1_sb", [P, MT])
        b2_sb = sb("b2_sb", [P, D])
        scale_sb = sb("scale_sb", [P, 1])

        scores = pb("scores", [P, 2, 2 * BANK])
        o_ps = pb("o_ps", [P, 2, BANK])
        work = pb("work", [P, 2, BANK])

        consts_in = sem("consts_in")
        b1_in = sem("b1_in")
        ident_zero, ident_made = sem("ident_zero"), sem("ident_made")
        stack_zeroed, v_ones_made = sem("stack_zeroed"), sem("v_ones_made")
        x_in, acc_in, w1_in, w2_in = sem("x_in"), sem("acc_in"), sem("w1_in"), sem("w2_in")
        stacks_in = [sem("stacks_in0"), sem("stacks_in1")]
        even_out, even_in, pair_out, out_stored = sem("even_out"), sem("even_in"), sem("pair_out"), sem("out_stored")
        scores_ready, exp_done, masked, pv_done = sem("scores_ready"), sem("exp_done"), sem("masked"), sem("pv_done")
        o_evac = [sem("o_evac0"), sem("o_evac1")]
        work_ready = sem("work_ready")
        work_free = [sem("work_free0"), sem("work_free1")]
        g_split = sem("g_split")
        w1_ready, w2_ready = sem("w1_ready"), sem("w2_ready")
        xn_ready, pair_ready, xt_split, v_ready = sem("xn_ready"), sem("pair_ready"), sem("xt_split"), sem("v_ready")
        acc_done = sem("acc_done")
        chain = sem("chain")

        block = ctx.enter_context(nc.Block())

        def over_sequences(eng, sequence):
            with eng.Fori(0, B - 1) as b:
                sequence(b, False)
            sequence(B - 1, True)

        def worked_out(eng, value):
            return value if isinstance(value, int) else eng.to_reg(value)

        @block.sync
        def _(sp):
            def load_x(b):
                sp.dma_start(xn[:, :, :], x[b, :, :].rearrange("(t p) d -> p t d", p=P)).then_inc(x_in, 16)

            def load_acc(b):
                sp.dma_start(acc[:, :, :], x[b, :, :].rearrange("(t p) d -> p t d", p=P)).then_inc(acc_in, 16)

            def exchange_even(b):
                sp.dma_start(even_dram[b, :, :], xn[1:1 + 4 * NLORA:2, 0, :]).then_inc(even_out, 16)
                sp.wait_ge(even_out, 16 * b + 16)
                sp.dma_start(even[:, :, :], even_dram[b, :, :].partition_broadcast(P)).then_inc(even_in, 16)

            def store_pair(b):
                for half in range(2):
                    for t in range(DT):
                        sp.dma_start(pair_dram[b, HEADS // DT * t:HEADS // DT * (t + 1), half, :, :],
                                     xt_pair[:, half, t, :]).then_inc(pair_out, 16)

            def load_stacks(b, g):
                for j in range(GH):
                    rows = slice(64 * (j % 2), 64 * (j % 2) + 4 * HD)
                    head = pair_dram[b, GH * g + j, :, :, :]
                    sp.dma_start(q_stack[rows, g % 2, j // 2, :],
                                 head.rearrange("a c s -> (a c) s").unsqueeze(0).broadcast_to([2, 2 * HD, S]))\
                      .then_inc(stacks_in[g % 2], 16)
                    for half in range(2):
                        rows = slice(64 * (j % 2) + 2 * HD * half, 64 * (j % 2) + 2 * HD * (half + 1))
                        sp.dma_start(k_stack[rows, g % 2, j, :],
                                     head[half, :, :].unsqueeze(0).broadcast_to([2, HD, S]))\
                          .then_inc(stacks_in[g % 2], 16)

            load_x(0)
            load_acc(0)
            sp.dma_start(scale_sb[:, :], scale.partition_broadcast(P)).then_inc(consts_in, 16)
            sp.dma_start(b2_sb[:, :], b2.partition_broadcast(P)).then_inc(consts_in, 16)
            sp.dma_start(b1_sb[:, :], b1).then_inc(b1_in, 16)
            sp.wait_ge(xn_ready, 1)
            exchange_even(0)
            sp.wait_ge(pair_ready, 1)
            store_pair(0)
            sp.wait_ge(pair_out, 16 * PAIR_DMAS)
            sp.wait_ge(stack_zeroed, 1)
            load_stacks(0, 0)

            def sequence(b, last):
                sp.wait_ge(xt_split, b + 1)
                sp.dma_start(w1[:, :, :], w1t.rearrange("(t p) h -> p t h", p=P)).then_inc(w1_in, 16)
                sp.dma_start(w2, w2t.rearrange("(t p) o -> p t o", p=P)).then_inc(w2_in, 16)
                sp.wait_ge(scores_ready, TILES * b + 1)
                load_stacks(b, 1)
                if not last:
                    sp.wait_ge(v_ready, GROUPS * b + GROUPS)
                    load_x(b + 1)
                sp.wait_ge(scores_ready, TILES * b + 2 * NS)
                load_stacks(b, 2)
                if not last:
                    used, normed = worked_out(sp, b + 1), worked_out(sp, b + 2)
                    sp.wait_ge(w2_ready, used)
                    sp.wait_ge(xn_ready, normed)
                    exchange_even(b + 1)
                sp.wait_ge(scores_ready, TILES * b + 4 * NS)
                load_stacks(b, 3)
                if not last:
                    sp.wait_ge(pair_ready, b + 2)
                    stored, scored = worked_out(sp, 16 * PAIR_DMAS * b + 32 * PAIR_DMAS), worked_out(sp, TILES * b + 6 * NS)
                    store_pair(b + 1)
                    sp.wait_ge(pair_out, stored)
                    sp.wait_ge(scores_ready, scored)
                    load_stacks(b + 1, 0)
                sp.wait_ge(acc_done, b + 1)
                sp.dma_start(out[b, :, :].rearrange("(t p) d -> p t d", p=P), acc[:, :, :]).then_inc(out_stored, 16)
                if not last:
                    sp.wait_ge(out_stored, 16 * b + 16)
                    load_acc(b + 1)

            over_sequences(sp, sequence)
            sp.wait_ge(out_stored, 16 * B)

        @block.gpsimd
        def _(pool):
            pool.memset(k_stack[:, :, :, :].rearrange("p a h s -> p (a h s)").bitcast(FP32), 0.0).then_inc(stack_zeroed, 1)
            pool.memset(ident[:, :], 0.0).then_inc(ident_zero, 1)
            pool.memset(v_ones[:, :, :, HD:HD + 1], 1.0)
            pool.memset(v_ones[:, :, :, HD + 1:VW], 0.0).then_inc(v_ones_made, 1)
            pool.wait_ge(ident_zero, 1)
            pool.affine_select(out=ident[:, :], in_=ident[:, :], compare_op=ALU.not_equal, fill=1.0, base=0,
                               pattern=[[-1, P]], channel_multiplier=1).then_inc(ident_made, 1)

            def mask(b, slot):
                i = slot % NS
                if not DIAG[i]:
                    return
                exps = worked_out(pool, TILES * b + 2 * slot + 2)
                pool.wait_ge(ident_made, 1)
                pool.wait_ge(exp_done, exps)
                for _, _, _, at, diagonal in columns(i):
                    if diagonal:
                        blk = probs[:, slot % RING, :, at:at + P]
                        last = pool.affine_select(out=blk, in_=blk, compare_op=ALU.is_ge, fill=0.0, base=0,
                                                  pattern=[[0, GH], [1, P]], channel_multiplier=-1)
                last.then_inc(masked, 1)

            for slot in range(LEAD):
                mask(0, slot)

            def sequence(b, last):
                for slot in range(LEAD, SLOTS_SEQ if last else SLOTS_SEQ + LEAD):
                    mask(b, slot)

            over_sequences(pool, sequence)

        @block.scalar
        def _(act):
            def exps(b, slot):
                for half in range(2):
                    act.wait_ge(scores_ready, TILES * b + 2 * slot + half + 1)
                    act.activation(probs[:, slot % RING, 2 * half:2 * half + 2, :].rearrange("p h q -> p (h q)"),
                                   scores[:, half, :], ACT.Exp, scale=EXP_SCALE).then_inc(exp_done, 1)

            def gelus(b, c):
                for m in range(MT):
                    use = use_of(b, "ffn1", c, m)
                    act.wait_ge(work_ready, USES_0 + USES * b + use + 1)
                    if m >= 2:
                        act.wait_ge(g_split, GELUS * b + MT * c + m - 1)
                    act.activation(gelu[:, m % 2, :], work[:, use % 2, :], ACT.Gelu,
                                   bias=b1_sb[:, m:m + 1]).then_inc(work_free[use % 2], 1)

            for slot in range(LEAD):
                exps(0, slot)
            act.wait_ge(b1_in, 16)

            def sequence(b, last):
                for slot in range(SLOTS_SEQ):
                    if not last or slot + LEAD < SLOTS_SEQ:
                        exps(b, slot + LEAD)
                    if slot in FFN1_AFTER:
                        gelus(b, FFN1_AFTER.index(slot))

            over_sequences(act, sequence)

        @block.tensor
        def _(pe):
            def bank_for(b, use):
                pe.wait_ge(work_free[use % 2], (USES_0 + USES * b) // 2 + use // 2 if isinstance(b, int)
                           else b * (USES // 2) + USES_0 // 2 + use // 2)
                return use % 2

            def score_tile(b, slot, half):
                g, i = slot // NS % GROUPS, slot % NS
                if i == 0 and half == 0:
                    loads = 16 * STACK_DMAS * (slot // NS // 2 + 1)
                    pe.wait_ge(stacks_in[g % 2], 2 * 16 * STACK_DMAS * b + loads)
                for j in (2 * half, 2 * half + 1):
                    for kb, q0, n, at, _ in columns(i):
                        last = pe.matmul(scores[:, half, (j % 2) * BANK + at:(j % 2) * BANK + at + n],
                                         k_stack[:, g % 2, j, kb * P:(kb + 1) * P],
                                         q_stack[:, g % 2, j // 2, q0:q0 + n], start=at == 0, stop=True,
                                         skip_group_check=True)
                last.then_inc(scores_ready, 1)

            def times_v(b, slot):
                g, i = slot // NS, slot % NS
                if i == 0:
                    pe.wait_ge(v_ready, GROUPS * b + g + 1)
                pe.wait_ge(exp_done, TILES * b + 2 * slot + 2)
                if DIAG[i]:
                    pe.wait_ge(masked, MASKS * b + masks_until(slot + 1))
                for kb, q0, n, at, _ in columns(i):
                    half = q0 // BANK
                    if kb == 0 and g:
                        pe.wait_ge(o_evac[half], GROUPS * b + g)
                    for j in range(GH):
                        last = pe.matmul(o_ps[VW * j:VW * (j + 1), half, q0 % BANK:q0 % BANK + n],
                                         v_ones[:, kb, GH * g + j, :], probs[:, slot % RING, j, at:at + n],
                                         start=kb == 0, stop=True, skip_group_check=True)
                last.then_inc(pv_done, 1)

            def ffn1(b, c):
                tok = slice(CHUNK * c, CHUNK * (c + 1))
                if c == 0:
                    pe.wait_ge(w1_ready, b + 1)
                    pe.wait_ge(xt_split, b + 1)
                for m in range(MT):
                    hid = slice(P * m, P * (m + 1))
                    bank = bank_for(b, use_of(b, "ffn1", c, m))
                    passes = [(w, xx, t) for t in range(DT) for w, xx in ((w1_hi, xt_hi), (w1_hi, xt_lo), (w1_lo, xt_hi))]
                    for n, (w, xx, t) in enumerate(passes):
                        last = pe.matmul(work[:, bank, :], w[:, t, hid], xx[:, t, tok],
                                         start=n == 0, stop=n == len(passes) - 1)
                    last.then_inc(work_ready, 1)

            def ffn2(b, c, tb):
                if tb == 0:
                    pe.wait_ge(w2_ready, b + 1)
                    pe.wait_ge(g_split, GELUS * b + MT * (c + 1))
                tok = slice(P * tb, P * (tb + 1))
                bank = bank_for(b, use_of(b, "ffn2", c, tb))
                passes = [(gg, w, m) for m in range(MT) for gg, w in ((g_hi, w2_hi), (g_hi, w2_lo), (g_lo, w2_hi))]
                for n, (gg, w, m) in enumerate(passes):
                    last = pe.matmul(work[:, bank, 0:D], gg[:, m, tok], w[:, m, :],
                                     start=n == 0, stop=n == len(passes) - 1)
                last.then_inc(work_ready, 1)

            def transpose_o(b, g, half):
                pe.wait_ge(o_evac[half], GROUPS * b + g + 1)
                bank = bank_for(b, use_of(b, "o", g, half))
                for t in range(TB):
                    last = pe.transpose(work[:, bank, P * t:P * (t + 1)], o_sb[:, half, P * t:P * (t + 1)], ident[:, :])
                last.then_inc(work_ready, 1)

            def transpose_xn(b, u):
                if isinstance(b, int) and b < 0:
                    bank = u % 2
                    if u >= 2:
                        pe.wait_ge(work_free[bank], u // 2)
                    pe.wait_ge(xn_ready, 1)
                else:
                    bank = bank_for(b, use_of(b, "xn", u))
                    pe.wait_ge(xn_ready, b + 2)
                for t in range(BANK // P):
                    last = pe.transpose(work[:, bank, P * t:P * (t + 1)],
                                        xn[:, 4 * (u % 2) + t, P * (u // 2):P * (u // 2 + 1)], ident[:, :])
                last.then_inc(work_ready, 1)

            pe.wait_ge(ident_made, 1)
            for u in range(XT_USES):
                transpose_xn(-1, u)
            for slot in range(LEAD):
                for half in range(2):
                    if slot:
                        pe.wait_ge(exp_done, 2 * slot + half - 1)
                    score_tile(0, slot, half)

            def sequence(b, last):
                for slot in range(SLOTS_SEQ):
                    ahead = slot + LEAD if not last or slot + LEAD < SLOTS_SEQ else None
                    for half in range(2):
                        if ahead is not None:
                            pe.wait_ge(exp_done, TILES * b + 2 * ahead + half - 1)
                            score_tile(b, ahead, half)
                        if half == 0:
                            times_v(b, slot)
                    for what, *arg in EXTRAS[slot]:
                        if what == "ffn1":
                            ffn1(b, *arg)
                        elif what == "ffn2":
                            ffn2(b, *arg)
                        elif what == "o":
                            transpose_o(b, *arg)
                        elif not last:
                            transpose_xn(b, *arg)

            over_sequences(pe, sequence)

        @block.vector
        def _(dve):
            steps = [0]

            def link(base, ins):
                steps[0] += 1
                ins.then_inc(chain, 1)
                dve.wait_ge(chain, base + steps[0])

            def layernorm(base, b):
                dve.wait_ge(x_in, 16 * b + 16)
                for t in range(NT):
                    ins = dve.bn_stats(stats[:, t, :], xn[:, t, :])
                steps[0] += 1
                ins.then_inc(chain, 1)
                count = worked_out(dve, base + steps[0])
                dve.wait_ge(v_ones_made, 1)
                dve.wait_ge(chain, count)
                for t in range(NT):
                    ins = dve.bn_aggr(mean_var[:, t, :], stats[:, t, :])
                link(base, ins)
                link(base, dve.tensor_scalar(var_eps[:, :, :], mean_var[:, :, 1:2], EPS, None, ALU.add))
                link(base, dve.tensor_scalar(newton[:, :, :].bitcast(I32), var_eps[:, :, :].bitcast(I32), 1, None,
                                             ALU.logical_shift_right))
                link(base, dve.tensor_scalar(rstd[:, :, :].bitcast(I32), newton[:, :, :].bitcast(I32), -1.0,
                                             float(0x5F3759DF), ALU.mult, ALU.add))
                for _ in range(3):
                    link(base, dve.scalar_tensor_tensor(newton[:, :, :], rstd[:, :, :], -0.5, rstd[:, :, :], ALU.mult, ALU.mult))
                    link(base, dve.tensor_tensor(newton[:, :, :], newton[:, :, :], var_eps[:, :, :], ALU.mult))
                    link(base, dve.scalar_tensor_tensor(rstd[:, :, :], newton[:, :, :], 1.5, rstd[:, :, :], ALU.add, ALU.mult))
                for t in range(NT):
                    ins = dve.tensor_scalar(xn[:, t, :], xn[:, t, :], mean_var[:, t, 0:1], rstd[:, t, :],
                                            ALU.subtract, ALU.mult)
                ins.then_inc(xn_ready, 1)

            def evac_xt(ready, u, bank):
                dve.wait_ge(work_ready, ready)
                dve.tensor_copy(xt[:, u // 2, BANK * (u % 2):BANK * (u % 2 + 1)], work[:, bank, :])\
                   .then_inc(work_free[bank], 1)

            def split_pair(base, b, free):
                dve.wait_ge(work_free[1], free)
                dve.wait_ge(work_free[0], free)
                if not (isinstance(b, int) and b == 0):
                    dve.wait_ge(pair_out, 16 * PAIR_DMAS * b)
                link(base, dve.tensor_scalar(xt_pair[:, 0, :, :], xt, QSCALE, None, ALU.mult))
                dve.scalar_tensor_tensor(xt_pair[:, 1, :, :], xt, QSCALE, xt_pair[:, 0, :, :], ALU.mult, ALU.subtract)\
                   .then_inc(pair_ready, 1)

            def split(base, hi, lo, full, done):
                link(base, dve.tensor_copy(hi, full))
                dve.tensor_tensor(lo, full, hi.bitcast(FP32), ALU.subtract).then_inc(done, 1)

            def split_xt(base):
                rows = xt[:, :, 2:2 + 4 * NLORA:2]
                dve.tensor_scalar(odd[:, :, :], rows, scale_sb[:, 0:1], None, ALU.mult)
                split(base, xt_hi[:, :, :], xt_lo[:, :, :], xt, xt_split)

            def copy_v(g):
                dve.tensor_copy(v_ones[:, :, GH * g:GH * (g + 1), 0:HD],
                                xn[:, :, GH * HD * g:GH * HD * (g + 1)].rearrange("p t (h d) -> p t h d", h=GH))\
                   .then_inc(v_ready, 1)

            def weights(base, b):
                dve.wait_ge(w1_in, 16 * b + 16)
                dve.wait_ge(even_in, 16 * b + 16)
                for t in range(DT):
                    for i in range(NLORA):
                        part = w1[:, t, D * i:D * (i + 1)]
                        ins = dve.scalar_tensor_tensor(part, even[:, i, :], odd[:, t, i:i + 1], part, ALU.mult, ALU.add)
                link(base, ins)
                split(base, w1_hi[:, :, :], w1_lo[:, :, :], w1[:, :, :], w1_ready)
                dve.wait_ge(w2_in, 16 * b + 16)
                step = HID // D
                cols = D // NLORA
                w2_v = w2.rearrange("p (c t) o -> p c t o", t=DT)
                for t in range(DT):
                    for i in range(NLORA):
                        part = w2_v[:, :, t, cols * i:cols * (i + 1)]
                        ins = dve.scalar_tensor_tensor(
                            part, even[:, NLORA + i, :].rearrange("p (a c) -> p c a", c=step),
                            odd[:, t, NLORA + i:NLORA + i + 1], part, ALU.mult, ALU.add)
                link(base, ins)
                split(base, w2_hi[:, :, :], w2_lo[:, :, :], w2, w2_ready)

            def evac_o(b, g, half):
                slots = NS * g + (HALF0_DONE if half == 0 else NS)
                dve.wait_ge(pv_done, SLOTS_SEQ * b + slots)
                dve.tensor_copy(o_sb[:, half, :], o_ps[:, half, :]).then_inc(o_evac[half], 1)

            def add_o(base, b, g, half):
                use = use_of(b, "o", g, half)
                dve.wait_ge(work_ready, USES_0 + USES * b + use + 1)
                o_t = work[:, use % 2, :].rearrange("p (t h c) -> p t h c", t=TB, h=GH)
                link(base, dve.reciprocal(rden[:, :, :, :], o_t[:, :, :, HD:HD + 1]))
                norm = o_norm[:, :, :].rearrange("p t (h c) -> p t h c", h=GH)
                ins = dve.tensor_tensor(norm, o_t[:, :, :, 0:HD], rden[:, :, :, :].broadcast_to([P, TB, GH, HD]), ALU.mult)
                ins.then_inc(work_free[use % 2], 1)
                dve.wait_ge(work_free[use % 2], freed(b, use))
                part = acc[:, TB * half:TB * (half + 1), GH * HD * g:GH * HD * (g + 1)]
                return dve.tensor_tensor(part, part, o_norm[:, :, :], ALU.add)

            def freed(b, use):
                return b * (USES // 2) + (USES_0 // 2 + use // 2 + 1)

            def split_gelu(base, b, c):
                for m in range(MT):
                    use = use_of(b, "ffn1", c, m)
                    dve.wait_ge(work_free[use % 2], freed(b, use))
                    split(base, g_hi[:, m, :], g_lo[:, m, :], gelu[:, m % 2, :], g_split)

            def add_ffn(b, c, tb):
                use = use_of(b, "ffn2", c, tb)
                dve.wait_ge(work_ready, USES_0 + USES * b + use + 1)
                part = acc[:, TB * c + tb, :]
                dve.tensor_tensor(part, part, work[:, use % 2, 0:D], ALU.add).then_inc(work_free[use % 2], 1)
                dve.wait_ge(work_free[use % 2], freed(b, use))

            layernorm(0, 0)
            for u in range(XT_USES):
                evac_xt(u + 1, u, u % 2)
            split_pair(0, 0, XT_USES // 2)
            dve.wait_ge(xn_ready, 1)
            for g in range(GROUPS):
                copy_v(g)
            dve.wait_ge(consts_in, 32)
            split_xt(0)
            assert steps[0] == CHAIN_0, steps[0]

            def sequence(b, last):
                steps[0] = 0
                base = CHAIN_0 + CHAIN * b
                dve.wait_ge(xt_split, b + 1)
                weights(base, b)
                dve.wait_ge(acc_in, 16 * b + 16)
                link(base, dve.tensor_tensor(acc[:, :, :], acc[:, :, :], b2_sb[:, :].unsqueeze(1).broadcast_to([P, NT, D]), ALU.add))
                for g in range(GROUPS):
                    c = g // 2
                    if g % 2:
                        for tb in range(2):
                            add_ffn(b, c, tb)
                    if g:
                        link(base, add_o(base, b, g - 1, 1))
                    if g % 2:
                        for tb in range(2, TB if g == 1 else TB - 1):
                            add_ffn(b, c, tb)
                    if g == 2 and not last:
                        for u in range(XT_USES):
                            use = use_of(b, "xn", u)
                            if u == 2:
                                evac_o(b, g, 0)
                            evac_xt(USES_0 + USES * b + use + 1, u, use % 2)
                        split_pair(base, b + 1, freed(b, use_of(b, "xn", XT_USES - 1)))
                    else:
                        evac_o(b, g, 0)
                    if g == 1 and not last:
                        layernorm(base, b + 1)
                    if g == 3 and not last:
                        split_xt(base)
                        dve.wait_ge(xn_ready, b + 2)
                        for gg in range(GROUPS - 1):
                            copy_v(gg)
                    link(base, add_o(base, b, g, 0))
                    evac_o(b, g, 1)
                    if g % 2 == 0:
                        split_gelu(base, b, c)
                if not last:
                    copy_v(GROUPS - 1)
                add_ffn(b, FFN_CHUNKS - 1, TB - 1)
                add_o(base, b, GROUPS - 1, 1).then_inc(acc_done, 1)
                assert last or steps[0] == CHAIN, steps[0]

            over_sequences(dve, sequence)


FFN1_AFTER = [NS - 1, 3 * NS - 1]
EXTRAS = [[] for _ in range(SLOTS_SEQ)]
for _g in range(GROUPS):
    EXTRAS[NS * _g + 6].append(("o", _g, 0))
    if _g:
        EXTRAS[NS * _g + 2].append(("o", _g - 1, 1))
for _c, _s in enumerate(FFN1_AFTER):
    EXTRAS[_s].append(("ffn1", _c))
    for _t in range(TB):
        EXTRAS[min(_s + 1 + _t, _s + NS) if _c == 0 or _t < TB - 1 else SLOTS_SEQ - 1].append(("ffn2", _c, _t))
for _u, _i in enumerate((2, 3, 4, 5)):
    EXTRAS[2 * NS + _i].append(("xn", _u))
EXTRAS[SLOTS_SEQ - 1].append(("o", GROUPS - 1, 1))


def _uses():
    order = []
    for extras in EXTRAS:
        for what, *arg in extras:
            order += [("ffn1", *arg, m) for m in range(MT)] if what == "ffn1" else [(what, *arg)]
    return order


USE = {last: {key: n for n, key in enumerate(k for k in _uses() if not (last and k[0] == "xn"))} for last in (False, True)}
assert len(USE[False]) == USES and USES % 2 == 0 and USES_0 % 2 == 0


def use_of(b, *key):
    return USE[isinstance(b, int) and b == B - 1][key]


def kernel(**inputs):
    import numpy as np
    import concourse.bacc as bacc
    from concourse.bass_utils import run_bass_kernel_spmd

    nc = bacc.Bacc("TRN2", target_bir_lowering=False, num_devices=1)
    arrays = {
        "x": np.ascontiguousarray(inputs["L0_attn_x"]),
        "w1t": np.ascontiguousarray(np.transpose(inputs["L0_ffn_W1"])),
        "w2t": np.ascontiguousarray(np.transpose(inputs["L0_ffn_W2"])),
        "b1": np.ascontiguousarray(np.transpose(np.reshape(inputs["L0_ffn_b1"], (MT, P)))),
        "b2": np.reshape(inputs["L0_ffn_b2"], (D,)),
        "scale": np.reshape(inputs["L0_ffn_scale"], (1,)),
    }
    args = [nc.dram_tensor(n, a.shape, mybir.dt.from_np(a.dtype), kind="ExternalInput").ap() for n, a in arrays.items()]
    args.append(nc.dram_tensor("out", (B, S, D), FP32, kind="ExternalOutput").ap())
    attention_ffn(nc, *args)
    r = run_bass_kernel_spmd(nc, [arrays], core_ids=[0])
    return r.results[0]["out"]
```

```python
from contextlib import ExitStack

import concourse.bass as bass
from concourse import mybir

FP32 = mybir.dt.float32
FP32R = mybir.dt.float32r
FP16 = mybir.dt.float16
I32 = mybir.dt.int32
ALU = mybir.AluOpType
ACT = mybir.ActivationFunctionType

B, S, D, HID = 8, 1024, 256, 1024
P = 128
HEADS, HD = 16, 16
NT = S // P
DT = D // P
MT = HID // P
BANK = 512
GH = 4
GROUPS = HEADS // GH
VW = 32
QSCALE = 1024.0
EXP_SCALE = HD ** -0.5 / QSCALE ** 2
EPS = 1e-5
CHUNK = 512
NLORA = 4

SLOTS = [
    [(0, 0, 512)],
    [(1, 128, 384), (3, 384, 128)],
    [(0, 512, 512)],
    [(2, 256, 256), (6, 768, 256)],
    [(1, 512, 512)],
    [(4, 512, 512)],
    [(2, 512, 512)],
    [(5, 640, 384), (7, 896, 128)],
    [(3, 512, 512)],
]
NS = len(SLOTS)
HALF0_DONE = 4
SLOTS_SEQ = NS * GROUPS
LEAD = 2
RING = 3
assert all(sum(n for _, _, n in segs) == BANK for segs in SLOTS)
assert sum(n for segs in SLOTS for _, _, n in segs) == sum(S - P * kb for kb in range(NT))


def columns(slot):
    at = 0
    for kb, q0, n in SLOTS[slot]:
        yield kb, q0, n, at, q0 == kb * P
        at += n


DIAG = [any(c[4] for c in columns(i)) for i in range(NS)]
DIAG_BEFORE = [sum(DIAG[:i]) for i in range(NS + 1)]
DIAG_GROUP = DIAG_BEFORE[NS]


def masks_until(slot):
    return slot // NS * DIAG_GROUP + DIAG_BEFORE[slot % NS]


TILES_0, TILES = 2 * LEAD, 2 * SLOTS_SEQ
MASKS_0, MASKS = masks_until(LEAD), DIAG_GROUP * GROUPS
FFN_CHUNKS = S // CHUNK
XT_USES = 4
TB = CHUNK // P
USES_0 = XT_USES
USES = FFN_CHUNKS * (MT + TB) + 2 * GROUPS + XT_USES
GELUS = FFN_CHUNKS * MT
STACK_DMAS = 1 + GH
STORE_DMAS = 3
HEAD_ROWS = 4 * HD
CONST_DMAS = 3
CHAIN = 53
CHAIN_0 = 22


def attention_ffn(nc, x, w1t, w2t, b1, b2, scale, out):
    ctx = ExitStack()
    with ctx:
        def sb(name, shape, dt=FP32):
            return ctx.enter_context(nc.sbuf_tensor(name, shape, dt))

        def pb(name, shape):
            return ctx.enter_context(nc.psum_tensor(name, shape, FP32))

        def sem(name):
            return ctx.enter_context(nc.semaphore(name))

        k_dram = nc.dram_tensor("k_dram", [B, HEADS, HD, 2, S], FP16, kind="Internal").ap()
        q_dram = nc.dram_tensor("q_dram", [B, HEADS, HD, 2, 2, S], FP16, kind="Internal").ap()
        even_dram = nc.dram_tensor("even_dram", [B, 2 * NLORA, D], FP32, kind="Internal").ap()

        q_stack = sb("q_stack", [P, 2, 2, S], FP16)
        k_stack = sb("k_stack", [P, 2, GH, S], FP16)
        probs = sb("probs", [P, RING, GH, BANK])
        v_ones = sb("v_ones", [P, NT, HEADS, VW])
        xn = sb("xn", [P, NT, D])
        xt_w2 = sb("xt_w2", [P, DT * S])
        xt = xt_w2[:, :].rearrange("p (t s) -> p t s", t=DT)
        w2 = xt_w2[:, :].rearrange("p (t o) -> p t o", t=MT)
        w1 = sb("w1", [P, DT, HID])
        xt_hi = sb("xt_hi", [P, DT, S], FP32R)
        xt_lo = sb("xt_lo", [P, DT, S], FP32R)
        xt_pair = sb("xt_pair", [P, 2, DT, S], FP16)
        w1_hi = sb("w1_hi", [P, DT, HID], FP32R)
        w1_lo = sb("w1_lo", [P, DT, HID], FP32R)
        w2_hi = sb("w2_hi", [P, MT, D], FP32R)
        w2_lo = sb("w2_lo", [P, MT, D], FP32R)
        gelu = sb("gelu", [P, 2, CHUNK])
        g_hi = sb("g_hi", [P, MT, CHUNK], FP32R)
        g_lo = sb("g_lo", [P, MT, CHUNK], FP32R)
        even = sb("even", [P, 2 * NLORA, D])
        odd = sb("odd", [P, DT, 2 * NLORA])
        acc = sb("acc", [P, NT, D])
        o_sb = sb("o_sb", [P, 2, BANK])
        rden = sb("rden", [P, TB, GH, 1])
        o_norm = sb("o_norm", [P, TB, GH * HD])
        stats = sb("stats", [P, NT, 6])
        mean_var = sb("mean_var", [P, NT, 2])
        var_eps = sb("var_eps", [P, NT, 1])
        rstd = sb("rstd", [P, NT, 1])
        newton = sb("newton", [P, NT, 1])
        ident = sb("ident", [P, P])
        b1_sb = sb("b1_sb", [P, MT])
        b2_sb = sb("b2_sb", [P, D])
        scale_sb = sb("scale_sb", [P, 1])

        scores = pb("scores", [P, 2, 2 * BANK])
        o_ps = pb("o_ps", [P, 2, BANK])
        work = pb("work", [P, 2, BANK])

        consts_in = sem("consts_in")
        b1_in = sem("b1_in")
        ident_zero, ident_made = sem("ident_zero"), sem("ident_made")
        stack_zeroed, v_ones_made = sem("stack_zeroed"), sem("v_ones_made")
        x_in = [sem("x_in0"), sem("x_in1")]
        acc_in, w1_in, w2_in = sem("acc_in"), sem("w1_in"), sem("w2_in")
        stacks_in = [sem("stacks_in0"), sem("stacks_in1")]
        even_out, even_in, out_stored = sem("even_out"), sem("even_in"), sem("out_stored")
        group0_out, xn_half_ready = sem("group0_out"), sem("xn_half_ready")
        pair_out = [sem(f"pair_out{t}") for t in range(DT)]
        scores_ready, exp_done, masked, pv_done = sem("scores_ready"), sem("exp_done"), sem("masked"), sem("pv_done")
        o_evac = [sem("o_evac0"), sem("o_evac1")]
        work_ready = sem("work_ready")
        work_free = [sem("work_free0"), sem("work_free1")]
        g_split = sem("g_split")
        w1_ready, w2_ready = sem("w1_ready"), sem("w2_ready")
        xn_ready, pair_ready, xt_split, v_ready = sem("xn_ready"), sem("pair_ready"), sem("xt_split"), sem("v_ready")
        acc_done = sem("acc_done")
        chain = sem("chain")

        block = ctx.enter_context(nc.Block())

        def over_sequences(eng, sequence):
            with eng.Fori(0, B - 1) as b:
                sequence(b, False)
            sequence(B - 1, True)

        def worked_out(eng, value):
            return value if isinstance(value, int) else eng.to_reg(value)

        @block.sync
        def _(sp):
            def load_x(b):
                for half in range(2):
                    blocks = slice(NT // 2 * half, NT // 2 * (half + 1))
                    sp.dma_start(xn[:, blocks, :], x[b, :, :].rearrange("(t p) d -> p t d", p=P)[:, blocks, :])\
                      .then_inc(x_in[half], 16)

            def load_acc(b, half):
                blocks = slice(TB * half, TB * (half + 1))
                sp.dma_start(acc[:, blocks, :], x[b, :, :].rearrange("(t p) d -> p t d", p=P)[:, blocks, :])\
                  .then_inc(acc_in, 16)

            def store_acc(b, half):
                blocks = slice(TB * half, TB * (half + 1))
                sp.wait_ge(acc_done, 2 * b + half + 1)
                sp.dma_start(out[b, :, :].rearrange("(t p) d -> p t d", p=P)[:, blocks, :], acc[:, blocks, :])\
                  .then_inc(out_stored, 16)

            def load_w1():
                sp.dma_start(w1[:, :, :], w1t.rearrange("(t p) h -> p t h", p=P)).then_inc(w1_in, 16)

            def load_w2():
                sp.dma_start(w2, w2t.rearrange("(t p) o -> p t o", p=P)).then_inc(w2_in, 16)

            def store_even(b):
                sp.dma_start(even_dram[b, :, :], xn[1:1 + 4 * NLORA:2, 0, :]).then_inc(even_out, 16)

            def load_even(b):
                sp.wait_ge(even_out, 16 * b + 16)
                sp.dma_start(even[:, :, :], even_dram[b, :, :].partition_broadcast(P)).then_inc(even_in, 16)

            def store_heads(b, first, count, done):
                t, row = first * HD // P, first * HD % P
                heads, rows = slice(first, first + count), slice(row, row + count * HD)
                sp.dma_start(k_dram[b, heads, :, :, :].rearrange("h c a s -> (h c) a s"),
                             xt_pair[rows, :, t, :]).then_inc(done, 16)
                for half in range(2):
                    sp.dma_start(q_dram[b, heads, :, :, half, :].rearrange("h c a s -> (h c) a s"),
                                 xt_pair[rows, half, t, :].unsqueeze(1).broadcast_to([count * HD, 2, S]))\
                      .then_inc(done, 16)

            def store_pair(b, t):
                store_heads(b, HEADS // DT * t, HEADS // DT, pair_out[t])

            def load_stacks(b, g):
                sp.dma_start(q_stack[:, g % 2, :, :],
                             q_dram[b, GH * g:GH * (g + 1), :, :, :, :].rearrange("(u h) c a e s -> (h c a e) u s", h=2))\
                  .then_inc(stacks_in[g % 2], 16)
                for j in range(GH):
                    sp.dma_start(k_stack[HEAD_ROWS * (j % 2):HEAD_ROWS * (j % 2 + 1), g % 2, j, :],
                                 k_dram[b, GH * g + j, :, :, :].rearrange("c a s -> (c a) s").unsqueeze(1)
                                 .broadcast_to([2 * HD, 2, S])).then_inc(stacks_in[g % 2], 16)

            load_x(0)
            sp.dma_start(scale_sb[:, :], scale.partition_broadcast(P)).then_inc(consts_in, 16)
            sp.dma_start(b2_sb[:, :], b2.partition_broadcast(P)).then_inc(consts_in, 16)
            sp.dma_start(b1_sb[:, :], b1).then_inc(b1_in, 16)
            load_w1()
            sp.wait_ge(xn_ready, 1)
            store_even(0)
            sp.wait_ge(pair_ready, 1)
            store_heads(0, 0, GH, group0_out)
            sp.wait_ge(group0_out, 16 * STORE_DMAS)
            sp.wait_ge(stack_zeroed, 1)
            load_stacks(0, 0)
            load_even(0)
            sp.wait_ge(xt_split, 1)
            load_w2()
            for half in range(2):
                load_acc(0, half)
            store_heads(0, GH, GH, pair_out[0])
            for t in range(1, DT):
                sp.wait_ge(pair_ready, t + 1)
                store_pair(0, t)
            sp.wait_ge(pair_out[0], 16 * STORE_DMAS)
            load_stacks(0, 1)
            for t in range(1, DT):
                sp.wait_ge(pair_out[t], 16 * STORE_DMAS)

            def sequence(b, last):
                if not last:
                    sp.wait_ge(v_ready, GROUPS * b + GROUPS)
                    load_x(b + 1)
                sp.wait_ge(scores_ready, TILES * b + 2 * NS)
                load_stacks(b, 2)
                if not last:
                    used, normed = worked_out(sp, b + 1), worked_out(sp, b + 2)
                    sp.wait_ge(w2_ready, used)
                    sp.wait_ge(xn_ready, normed)
                    store_even(b + 1)
                    load_even(b + 1)
                    load_w1()
                sp.wait_ge(scores_ready, TILES * b + 4 * NS)
                load_stacks(b, 3)
                if not last:
                    stored, scored = worked_out(sp, 16 * STORE_DMAS * b + 32 * STORE_DMAS), worked_out(sp, TILES * b + 6 * NS)
                    for t in range(DT):
                        sp.wait_ge(pair_ready, DT * b + DT + t + 1)
                        store_pair(b + 1, t)
                    for t in range(DT):
                        sp.wait_ge(pair_out[t], stored)
                    sp.wait_ge(scores_ready, scored)
                    load_stacks(b + 1, 0)
                    sp.wait_ge(xt_split, b + 2)
                    load_w2()
                    sp.wait_ge(scores_ready, TILES * b + TILES + 1)
                    load_stacks(b + 1, 1)
                for half in range(2):
                    store_acc(b, half)
                    if not last:
                        sp.wait_ge(out_stored, 32 * b + 16 * half + 16)
                        load_acc(b + 1, half)

            over_sequences(sp, sequence)
            sp.wait_ge(out_stored, 32 * B)

        @block.gpsimd
        def _(pool):
            pool.memset(k_stack[:, :, :, :].rearrange("p a h s -> p (a h s)").bitcast(FP32), 0.0).then_inc(stack_zeroed, 1)
            pool.memset(ident[:, :], 0.0).then_inc(ident_zero, 1)
            pool.memset(v_ones[:, :, :, HD:HD + 1], 1.0)
            pool.memset(v_ones[:, :, :, HD + 1:VW], 0.0).then_inc(v_ones_made, 1)
            pool.wait_ge(ident_zero, 1)
            pool.affine_select(out=ident[:, :], in_=ident[:, :], compare_op=ALU.not_equal, fill=1.0, base=0,
                               pattern=[[-1, P]], channel_multiplier=1).then_inc(ident_made, 1)

            def mask(b, slot):
                i = slot % NS
                if not DIAG[i]:
                    return
                exps = worked_out(pool, TILES * b + 2 * slot + 2)
                pool.wait_ge(ident_made, 1)
                pool.wait_ge(exp_done, exps)
                for _, _, _, at, diagonal in columns(i):
                    if diagonal:
                        blk = probs[:, slot % RING, :, at:at + P]
                        last = pool.affine_select(out=blk, in_=blk, compare_op=ALU.is_ge, fill=0.0, base=0,
                                                  pattern=[[0, GH], [1, P]], channel_multiplier=-1)
                last.then_inc(masked, 1)

            for slot in range(LEAD):
                mask(0, slot)

            def sequence(b, last):
                for slot in range(LEAD, SLOTS_SEQ if last else SLOTS_SEQ + LEAD):
                    mask(b, slot)

            over_sequences(pool, sequence)

        @block.scalar
        def _(act):
            def exps(b, slot):
                for half in range(2):
                    act.wait_ge(scores_ready, TILES * b + 2 * slot + half + 1)
                    act.activation(probs[:, slot % RING, 2 * half:2 * half + 2, :].rearrange("p h q -> p (h q)"),
                                   scores[:, half, :], ACT.Exp, scale=EXP_SCALE).then_inc(exp_done, 1)

            def gelus(b, c):
                for m in range(MT):
                    use = use_of(b, "ffn1", c, m)
                    act.wait_ge(work_ready, USES_0 + USES * b + use + 1)
                    if m >= 2:
                        act.wait_ge(g_split, GELUS * b + MT * c + m - 1)
                    act.activation(gelu[:, m % 2, :], work[:, use % 2, :], ACT.Gelu,
                                   bias=b1_sb[:, m:m + 1]).then_inc(work_free[use % 2], 1)

            for slot in range(LEAD):
                exps(0, slot)
            act.wait_ge(b1_in, 16)

            def sequence(b, last):
                for slot in range(SLOTS_SEQ):
                    if not last or slot + LEAD < SLOTS_SEQ:
                        exps(b, slot + LEAD)
                    if slot in FFN1_AFTER:
                        gelus(b, FFN1_AFTER.index(slot))

            over_sequences(act, sequence)

        @block.tensor
        def _(pe):
            def bank_for(b, use):
                pe.wait_ge(work_free[use % 2], (USES_0 + USES * b) // 2 + use // 2 if isinstance(b, int)
                           else b * (USES // 2) + USES_0 // 2 + use // 2)
                return use % 2

            def score_tile(b, slot, half):
                g, i = slot // NS % GROUPS, slot % NS
                if i == 0 and half == 0:
                    loads = 16 * STACK_DMAS * (slot // NS // 2 + 1)
                    pe.wait_ge(stacks_in[g % 2], 2 * 16 * STACK_DMAS * b + loads)
                for j in (2 * half, 2 * half + 1):
                    for kb, q0, n, at, _ in columns(i):
                        last = pe.matmul(scores[:, half, (j % 2) * BANK + at:(j % 2) * BANK + at + n],
                                         k_stack[:, g % 2, j, kb * P:(kb + 1) * P],
                                         q_stack[:, g % 2, j // 2, q0:q0 + n], start=at == 0, stop=True,
                                         skip_group_check=True)
                last.then_inc(scores_ready, 1)

            def times_v(b, slot):
                g, i = slot // NS, slot % NS
                if i == 0:
                    pe.wait_ge(v_ready, GROUPS * b + g + 1)
                pe.wait_ge(exp_done, TILES * b + 2 * slot + 2)
                if DIAG[i]:
                    pe.wait_ge(masked, MASKS * b + masks_until(slot + 1))
                for kb, q0, n, at, _ in columns(i):
                    half = q0 // BANK
                    if kb == 0 and g:
                        pe.wait_ge(o_evac[half], GROUPS * b + g)
                    for j in range(GH):
                        last = pe.matmul(o_ps[VW * j:VW * (j + 1), half, q0 % BANK:q0 % BANK + n],
                                         v_ones[:, kb, GH * g + j, :], probs[:, slot % RING, j, at:at + n],
                                         start=kb == 0, stop=True, skip_group_check=True)
                last.then_inc(pv_done, 1)

            def ffn1(b, c):
                tok = slice(CHUNK * c, CHUNK * (c + 1))
                if c == 0:
                    pe.wait_ge(w1_ready, b + 1)
                    pe.wait_ge(xt_split, b + 1)
                for m in range(MT):
                    hid = slice(P * m, P * (m + 1))
                    bank = bank_for(b, use_of(b, "ffn1", c, m))
                    passes = [(w, xx, t) for t in range(DT) for w, xx in ((w1_hi, xt_hi), (w1_hi, xt_lo), (w1_lo, xt_hi))]
                    for n, (w, xx, t) in enumerate(passes):
                        last = pe.matmul(work[:, bank, :], w[:, t, hid], xx[:, t, tok],
                                         start=n == 0, stop=n == len(passes) - 1)
                    last.then_inc(work_ready, 1)

            def ffn2(b, c, tb, part):
                if tb == 0 and part == 0:
                    pe.wait_ge(w2_ready, b + 1)
                    pe.wait_ge(g_split, GELUS * b + MT * (c + 1))
                tok = slice(P * tb, P * (tb + 1))
                bank = bank_for(b, use_of(b, "ffn2", c, tb)) if part == 0 else use_of(b, "ffn2", c, tb) % 2
                passes = [(gg, w, m) for m in range(MT) for gg, w in ((g_hi, w2_hi), (g_hi, w2_lo), (g_lo, w2_hi))]
                for n in range(len(passes) // 2 * part, len(passes) // 2 * (part + 1)):
                    gg, w, m = passes[n]
                    last = pe.matmul(work[:, bank, 0:D], gg[:, m, tok], w[:, m, :],
                                     start=n == 0, stop=n == len(passes) - 1)
                if part == 1:
                    last.then_inc(work_ready, 1)

            def transpose_o(b, g, half):
                pe.wait_ge(o_evac[half], GROUPS * b + g + 1)
                bank = bank_for(b, use_of(b, "o", g, half))
                for t in range(TB):
                    last = pe.transpose(work[:, bank, P * t:P * (t + 1)], o_sb[:, half, P * t:P * (t + 1)], ident[:, :])
                last.then_inc(work_ready, 1)

            def transpose_xn(b, u):
                if isinstance(b, int) and b < 0:
                    bank = u % 2
                    if u >= 2:
                        pe.wait_ge(work_free[bank], u // 2)
                    if u == 0:
                        pe.wait_ge(xn_half_ready, 1)
                    else:
                        pe.wait_ge(xn_ready, 1)
                else:
                    bank = bank_for(b, use_of(b, "xn", u))
                    pe.wait_ge(xn_ready, b + 2)
                for t in range(BANK // P):
                    last = pe.transpose(work[:, bank, P * t:P * (t + 1)],
                                        xn[:, 4 * (u % 2) + t, P * (u // 2):P * (u // 2 + 1)], ident[:, :])
                last.then_inc(work_ready, 1)

            pe.wait_ge(ident_made, 1)
            for u in range(XT_USES):
                transpose_xn(-1, u)
            for slot in range(LEAD):
                for half in range(2):
                    if slot:
                        pe.wait_ge(exp_done, 2 * slot + half - 1)
                    score_tile(0, slot, half)

            def sequence(b, last):
                for slot in range(SLOTS_SEQ):
                    ahead = slot + LEAD if not last or slot + LEAD < SLOTS_SEQ else None
                    for half in range(2):
                        if ahead is not None:
                            pe.wait_ge(exp_done, TILES * b + 2 * ahead + half - 1)
                            score_tile(b, ahead, half)
                        if half == (slot in FFN1_AFTER):
                            times_v(b, slot)
                    for what, *arg in EXTRAS[slot]:
                        if what == "ffn1":
                            ffn1(b, *arg)
                        elif what == "ffn2":
                            ffn2(b, *arg)
                        elif what == "o":
                            transpose_o(b, *arg)
                        elif not last:
                            transpose_xn(b, *arg)

            over_sequences(pe, sequence)

        @block.vector
        def _(dve):
            steps = [0]

            def link(base, ins):
                steps[0] += 1
                ins.then_inc(chain, 1)
                dve.wait_ge(chain, base + steps[0])

            def ln_stats(base, b):
                for t in range(NT):
                    if t % (NT // 2) == 0:
                        dve.wait_ge(x_in[t // (NT // 2)], 16 * b + 16)
                    ins = dve.bn_stats(stats[:, t, :], xn[:, t, :])
                steps[0] += 1
                ins.then_inc(chain, 1)
                count = worked_out(dve, base + steps[0])
                dve.wait_ge(v_ones_made, 1)
                dve.wait_ge(chain, count)
                for t in range(NT):
                    ins = dve.bn_aggr(mean_var[:, t, :], stats[:, t, :])
                link(base, ins)

            def ln_rstd(base):
                link(base, dve.tensor_scalar(var_eps[:, :, :], mean_var[:, :, 1:2], EPS, None, ALU.add))
                link(base, dve.tensor_scalar(newton[:, :, :].bitcast(I32), var_eps[:, :, :].bitcast(I32), 1, None,
                                             ALU.logical_shift_right))
                link(base, dve.tensor_scalar(rstd[:, :, :].bitcast(I32), newton[:, :, :].bitcast(I32), -1.0,
                                             float(0x5F3759DF), ALU.mult, ALU.add))
                for _ in range(3):
                    link(base, dve.scalar_tensor_tensor(newton[:, :, :], rstd[:, :, :], -0.5, rstd[:, :, :], ALU.mult, ALU.mult))
                    link(base, dve.tensor_tensor(newton[:, :, :], newton[:, :, :], var_eps[:, :, :], ALU.mult))
                    link(base, dve.scalar_tensor_tensor(rstd[:, :, :], newton[:, :, :], 1.5, rstd[:, :, :], ALU.add, ALU.mult))

            def ln_apply(half_ready=None):
                for t in range(NT):
                    if t == NT // 2 and half_ready is not None:
                        ins.then_inc(half_ready, 1)
                    ins = dve.tensor_scalar(xn[:, t, :], xn[:, t, :], mean_var[:, t, 0:1], rstd[:, t, :],
                                            ALU.subtract, ALU.mult)
                ins.then_inc(xn_ready, 1)

            def evac_xt(ready, u, bank):
                dve.wait_ge(work_ready, ready)
                dve.tensor_copy(xt[:, u // 2, BANK * (u % 2):BANK * (u % 2 + 1)], work[:, bank, :])\
                   .then_inc(work_free[bank], 1)

            def split_pair(base, b, t, free_before, free):
                for bank, count in (free_before, free):
                    dve.wait_ge(work_free[bank], count)
                dve.wait_ge(pair_out[t], 16 * STORE_DMAS * b)
                link(base, dve.tensor_scalar(xt_pair[:, 0, t, :], xt[:, t, :], QSCALE, None, ALU.mult))
                dve.scalar_tensor_tensor(xt_pair[:, 1, t, :], xt[:, t, :], QSCALE, xt_pair[:, 0, t, :],
                                         ALU.mult, ALU.subtract).then_inc(pair_ready, 1)

            def split(base, hi, lo, full, done):
                link(base, dve.tensor_copy(hi, full))
                dve.tensor_tensor(lo, full, hi.bitcast(FP32), ALU.subtract).then_inc(done, 1)

            def scale_odd(base):
                rows = xt[:, :, 2:2 + 4 * NLORA:2]
                link(base, dve.tensor_scalar(odd[:, :, :], rows, scale_sb[:, 0:1], None, ALU.mult))

            def split_xt(base):
                split(base, xt_hi[:, :, :], xt_lo[:, :, :], xt, xt_split)

            def copy_v(g):
                dve.tensor_copy(v_ones[:, :, GH * g:GH * (g + 1), 0:HD],
                                xn[:, :, GH * HD * g:GH * HD * (g + 1)].rearrange("p t (h d) -> p t h d", h=GH))\
                   .then_inc(v_ready, 1)

            def add_m1(base, b):
                dve.wait_ge(w1_in, 16 * b + 16)
                dve.wait_ge(even_in, 16 * b + 16)
                for t in range(DT):
                    for i in range(NLORA):
                        part = w1[:, t, D * i:D * (i + 1)]
                        ins = dve.scalar_tensor_tensor(part, even[:, i, :], odd[:, t, i:i + 1], part, ALU.mult, ALU.add)
                link(base, ins)
                split(base, w1_hi[:, :, :], w1_lo[:, :, :], w1[:, :, :], w1_ready)

            def add_m2(base, b):
                dve.wait_ge(w2_in, 16 * b + 16)
                step = HID // D
                cols = D // NLORA
                w2_v = w2.rearrange("p (c t) o -> p c t o", t=DT)
                for t in range(DT):
                    for i in range(NLORA):
                        part = w2_v[:, :, t, cols * i:cols * (i + 1)]
                        ins = dve.scalar_tensor_tensor(
                            part, even[:, NLORA + i, :].rearrange("p (a c) -> p c a", c=step),
                            odd[:, t, NLORA + i:NLORA + i + 1], part, ALU.mult, ALU.add)
                link(base, ins)
                split(base, w2_hi[:, :, :], w2_lo[:, :, :], w2, w2_ready)

            def evac_o(b, g, half):
                slots = NS * g + (HALF0_DONE if half == 0 else NS)
                dve.wait_ge(pv_done, SLOTS_SEQ * b + slots)
                dve.tensor_copy(o_sb[:, half, :], o_ps[:, half, :]).then_inc(o_evac[half], 1)

            def add_o(base, b, g, half):
                use = use_of(b, "o", g, half)
                dve.wait_ge(work_ready, USES_0 + USES * b + use + 1)
                o_t = work[:, use % 2, :].rearrange("p (t h c) -> p t h c", t=TB, h=GH)
                link(base, dve.reciprocal(rden[:, :, :, :], o_t[:, :, :, HD:HD + 1]))
                norm = o_norm[:, :, :].rearrange("p t (h c) -> p t h c", h=GH)
                ins = dve.tensor_tensor(norm, o_t[:, :, :, 0:HD], rden[:, :, :, :].broadcast_to([P, TB, GH, HD]), ALU.mult)
                ins.then_inc(work_free[use % 2], 1)
                dve.wait_ge(work_free[use % 2], freed(b, use))
                part = acc[:, TB * half:TB * (half + 1), GH * HD * g:GH * HD * (g + 1)]
                return dve.tensor_tensor(part, part, o_norm[:, :, :], ALU.add)

            def freed(b, use):
                return b * (USES // 2) + (USES_0 // 2 + use // 2 + 1)

            def split_gelu(base, b, c):
                for m in range(MT):
                    use = use_of(b, "ffn1", c, m)
                    dve.wait_ge(work_free[use % 2], freed(b, use))
                    split(base, g_hi[:, m, :], g_lo[:, m, :], gelu[:, m % 2, :], g_split)

            def add_ffn(b, c, tb):
                use = use_of(b, "ffn2", c, tb)
                dve.wait_ge(work_ready, USES_0 + USES * b + use + 1)
                part = acc[:, TB * c + tb, :]
                dve.tensor_tensor(part, part, work[:, use % 2, 0:D], ALU.add).then_inc(work_free[use % 2], 1)
                dve.wait_ge(work_free[use % 2], freed(b, use))

            ln_stats(0, 0)
            ln_rstd(0)
            ln_apply(xn_half_ready)
            for t in range(DT):
                for half in range(2):
                    dve.wait_ge(work_ready, 2 * t + half + 1)
                    tok = slice(BANK * half, BANK * (half + 1))
                    link(0, dve.tensor_scalar(xt_pair[:, 0, t, tok], work[:, half, :], QSCALE, None, ALU.mult))
                    ins = dve.scalar_tensor_tensor(xt_pair[:, 1, t, tok], work[:, half, :], QSCALE,
                                                   xt_pair[:, 0, t, tok], ALU.mult, ALU.subtract)
                ins.then_inc(pair_ready, 1)
                for half in range(2):
                    evac_xt(2 * t + half + 1, 2 * t + half, half)
            dve.wait_ge(xn_ready, 1)
            for g in range(GROUPS):
                copy_v(g)
            dve.wait_ge(consts_in, 32)
            for bank in range(2):
                dve.wait_ge(work_free[bank], DT)
            scale_odd(0)
            split_xt(0)
            add_m1(0, 0)
            assert steps[0] == CHAIN_0, steps[0]

            def sequence(b, last):
                steps[0] = 0
                base = CHAIN_0 + CHAIN * b
                dve.wait_ge(xt_split, b + 1)
                add_m2(base, b)
                for slot in range(SLOTS_SEQ):
                    g, i = slot // NS, slot % NS
                    if i == HALF0_DONE - 1:
                        evac_o(b, g, 0)
                    if i == NS - 1:
                        evac_o(b, g, 1)
                    if slot == SLOTS_SEQ - 1 and not last:
                        copy_v(GROUPS - 1)
                    for what, *arg in EXTRAS[slot]:
                        if what == "ffn1":
                            split_gelu(base, b, *arg)
                        elif what == "ffn2":
                            if arg[2] == 1:
                                add_ffn(b, *arg[:2])
                        elif what == "o":
                            total = add_o(base, b, *arg)
                            if arg[0] == GROUPS - 1:
                                total.then_inc(acc_done, 1)
                            else:
                                link(base, total)
                        elif not last:
                            use = use_of(b, "xn", *arg)
                            evac_xt(USES_0 + USES * b + use + 1, *arg, use % 2)
                            if arg[0] % 2:
                                before = use_of(b, "xn", arg[0] - 1)
                                split_pair(base, b + 1, arg[0] // 2, (before % 2, freed(b, before)), (use % 2, freed(b, use)))
                                if arg[0] == XT_USES - 1:
                                    scale_odd(base)
                    if slot == ADD_B2:
                        dve.wait_ge(acc_in, 32 * b + 32)
                        link(base, dve.tensor_tensor(acc[:, :, :], acc[:, :, :],
                                                     b2_sb[:, :].unsqueeze(1).broadcast_to([P, NT, D]), ALU.add))
                    if not last:
                        if slot == LN_STATS:
                            ln_stats(base, b + 1)
                        if slot == LN_RSTD:
                            ln_rstd(base)
                        if slot == LN_APPLY:
                            ln_apply()
                        if slot == SPLIT_XT:
                            split_xt(base)
                        if slot == ADD_M1:
                            add_m1(base, b + 1)
                        if slot == COPY_V:
                            for gg in range(GROUPS - 1):
                                copy_v(gg)
                assert last or steps[0] == CHAIN, steps[0]

            over_sequences(dve, sequence)


EXTRAS_AFTER = {
    3: [("ffn1", 0)], 4: [("ffn2", 0, 0, 0)], 6: [("ffn2", 0, 0, 1), ("o", 0, 0)], 7: [("ffn2", 0, 1, 0)],
    9: [("ffn2", 0, 1, 1), ("ffn2", 0, 2, 0)], 11: [("ffn2", 0, 2, 1)], 13: [("o", 0, 1)],
    15: [("ffn2", 0, 3, 0)], 16: [("ffn2", 0, 3, 1), ("ffn1", 1)], 17: [("xn", 0), ("xn", 1)],
    18: [("o", 1, 1)], 20: [("o", 1, 0)], 21: [("xn", 2)], 22: [("ffn2", 1, 0, 0)],
    24: [("ffn2", 1, 0, 1), ("xn", 3)], 25: [("ffn2", 1, 1, 0), ("ffn2", 1, 1, 1)],
    27: [("o", 2, 0), ("o", 2, 1)], 29: [("ffn2", 1, 2, 0)], 30: [("ffn2", 1, 2, 1)], 32: [("o", 3, 0)],
    33: [("ffn2", 1, 3, 0)], 35: [("ffn2", 1, 3, 1), ("o", 3, 1)],
}
EXTRAS = [EXTRAS_AFTER.get(slot, []) for slot in range(SLOTS_SEQ)]
FFN1_AFTER = [slot for slot in range(SLOTS_SEQ) for extra in EXTRAS[slot] if extra[0] == "ffn1"]
ADD_B2 = 3
LN_STATS, LN_RSTD, LN_APPLY = 5, 7, 12
SPLIT_XT, ADD_M1, COPY_V = 29, 31, 29
POSITION = {extra: (slot, n) for slot in range(SLOTS_SEQ) for n, extra in enumerate(EXTRAS[slot])}
assert LN_APPLY < POSITION["xn", 0][0]
assert SPLIT_XT >= POSITION["xn", XT_USES - 1][0]
assert FFN1_AFTER[-1] < SPLIT_XT < ADD_M1
assert COPY_V >= NS * (GROUPS - 1) - 1
assert all(POSITION["ffn2", c, TB - 1, 1] < POSITION["o", GROUPS - 1, c] for c in range(FFN_CHUNKS))
for _g in range(GROUPS):
    assert HALF0_DONE - 1 <= POSITION["o", _g, 0][0] - NS * _g < NS + HALF0_DONE - 1
    assert NS - 1 <= POSITION["o", _g, 1][0] - NS * _g < 2 * NS - 1


def _uses():
    order = []
    for extras in EXTRAS:
        for what, *arg in extras:
            if what == "ffn1":
                order += [(what, *arg, m) for m in range(MT)]
            elif what != "ffn2" or arg[2] == 0:
                order.append((what, *arg[:2]))
    return order


USE = {last: {key: n for n, key in enumerate(k for k in _uses() if not (last and k[0] == "xn"))} for last in (False, True)}
assert len(USE[False]) == USES and USES % 2 == 0 and USES_0 % 2 == 0


def use_of(b, *key):
    return USE[isinstance(b, int) and b == B - 1][key]


def kernel(**inputs):
    import numpy as np
    import concourse.bacc as bacc
    from concourse.bass_utils import run_bass_kernel_spmd

    nc = bacc.Bacc("TRN2", target_bir_lowering=False, num_devices=1)
    arrays = {
        "x": np.ascontiguousarray(inputs["L0_attn_x"]),
        "w1t": np.ascontiguousarray(np.transpose(inputs["L0_ffn_W1"])),
        "w2t": np.ascontiguousarray(np.transpose(inputs["L0_ffn_W2"])),
        "b1": np.ascontiguousarray(np.transpose(np.reshape(inputs["L0_ffn_b1"], (MT, P)))),
        "b2": np.reshape(inputs["L0_ffn_b2"], (D,)),
        "scale": np.reshape(inputs["L0_ffn_scale"], (1,)),
    }
    args = [nc.dram_tensor(n, a.shape, mybir.dt.from_np(a.dtype), kind="ExternalInput").ap() for n, a in arrays.items()]
    args.append(nc.dram_tensor("out", (B, S, D), FP32, kind="ExternalOutput").ap())
    attention_ffn(nc, *args)
    r = run_bass_kernel_spmd(nc, [arrays], core_ids=[0])
    return r.results[0]["out"]
```
